# Optimizing a Trainium2 kernel written in Bass

```python
import numpy as np
import jax
import jax.numpy as jnp

def _softmax(x, axis=-1):
    return jax.nn.softmax(x, axis=axis)

def _gelu(x):
    return jax.nn.gelu(x, approximate=True)

def _silu(x):
    return jax.nn.silu(x)

def _sigmoid(x):
    return jax.nn.sigmoid(x)

def _layernorm(x, axis=-1, eps=1e-05):
    m = jnp.mean(x, axis=axis, keepdims=True)
    v = jnp.var(x, axis=axis, keepdims=True)
    return (x - m) / jnp.sqrt(v + eps)

def _scatter_add(tgt, idx, src, axis=0):
    return tgt.at[idx].add(src)

def _segment_sum(src, seg, n):
    return jax.ops.segment_sum(src, seg, n)
kernel_name = 'mk_lm_tower_d1_tok_ids256_r4_0626ef'

def setup_inputs(seed: int=0):
    np.random.seed(seed)
    _w = jnp.asarray

    def _rec_inputs():
        import jax
        import jax.numpy as jnp
        _rk = jax.random.key(seed)
        x = jax.random.randint(jax.random.fold_in(_rk, 1), (8, 256), 0, 12564, jnp.int32)
        return x
    x = _rec_inputs()

    def _L0_tok_setup():
        import jax, jax.numpy as jnp
        import numpy as np
        INP_SIZE = 50257
        HIDDEN = 64
        KSIZE = 9
        B, T = (16, 1024)
        key = jax.random.key(seed)
        k1, k2, k3, k4 = jax.random.split(key, 4)
        x = jax.random.randint(k1, (B, T), 0, INP_SIZE, dtype=jnp.int64 if jax.config.jax_enable_x64 else jnp.int32)
        emb = jax.random.normal(k2, (INP_SIZE, HIDDEN), dtype=jnp.float32) * 0.02
        fan_in = HIDDEN * KSIZE
        bound = 1.0 / np.sqrt(fan_in)
        W = jax.random.uniform(k3, (HIDDEN, HIDDEN, KSIZE), dtype=jnp.float32, minval=-bound, maxval=bound)
        b = jax.random.uniform(k4, (HIDDEN,), dtype=jnp.float32, minval=-bound, maxval=bound)
        return {'x': x, 'emb': emb, 'W': W, 'b': b}
    _L0_tok_all = _L0_tok_setup()
    _L0_tok_in = {k: v for k, v in _L0_tok_all.items() if k in ('emb', 'W', 'b')}
    del _L0_tok_all

    def _L0_attn_setup():
        import jax, jax.numpy as jnp
        import numpy as np
        B, S, I, H, O = (64, 128, 64, 256, 64)

        def _rnn_layer(inp, W_ih, W_hh, b_ih, b_hh):
            pre = jnp.einsum('bsi,hi->bsh', inp, W_ih) + (b_ih + b_hh)
            h0 = jnp.zeros((inp.shape[0], W_hh.shape[0]), dtype=inp.dtype)

            def step(h, p_t):
                h = jnp.tanh(p_t + h @ W_hh.T)
                return (h, h)
            _, hs = jax.lax.scan(step, h0, jnp.swapaxes(pre, 0, 1))
            return jnp.swapaxes(hs, 0, 1)
        key = jax.random.key(seed)
        ks = jax.random.split(key, 12)
        s_in = 1.0 / np.sqrt(H)
        inp = {'x': jax.random.normal(ks[0], (B, S, I), dtype=jnp.float32), 'W_ih_0': jax.random.uniform(ks[1], (H, I), jnp.float32, -s_in, s_in), 'W_hh_0': jax.random.uniform(ks[2], (H, H), jnp.float32, -s_in, s_in), 'b_ih_0': jax.random.uniform(ks[3], (H,), jnp.float32, -s_in, s_in), 'b_hh_0': jax.random.uniform(ks[4], (H,), jnp.float32, -s_in, s_in), 'W_ih_1': jax.random.uniform(ks[5], (H, H), jnp.float32, -s_in, s_in), 'W_hh_1': jax.random.uniform(ks[6], (H, H), jnp.float32, -s_in, s_in), 'b_ih_1': jax.random.uniform(ks[7], (H,), jnp.float32, -s_in, s_in), 'b_hh_1': jax.random.uniform(ks[8], (H,), jnp.float32, -s_in, s_in), 'fc_w': jax.random.uniform(ks[9], (O, H), jnp.float32, -s_in, s_in), 'fc_b': jax.random.uniform(ks[10], (O,), jnp.float32, -s_in, s_in)}
        return inp
    _L0_attn_all = _L0_attn_setup()
    _L0_attn_in = {k: v for k, v in _L0_attn_all.items() if k in ('W_ih_0', 'W_hh_0', 'b_ih_0', 'b_hh_0', 'W_ih_1', 'W_hh_1', 'b_ih_1', 'b_hh_1', 'fc_w', 'fc_b')}
    del _L0_attn_all

    def _L0_ffn_setup():
        import jax, jax.numpy as jnp
        import numpy as np
        NUM_EXPERTS = 8
        TOP_K = 2
        B, S, D = (8, 2048, 64)

        def _moe(tokens, router_w, w1, b1, w2, b2):
            N = tokens.shape[0]
            E = router_w.shape[0]
            logits = tokens.astype(jnp.float32) @ router_w.astype(jnp.float32).T
            probs = jax.nn.softmax(logits, axis=-1)
            rw, re = jax.lax.top_k(probs, TOP_K)
            if TOP_K > 1:
                rw = rw / jnp.maximum(rw.sum(-1, keepdims=True), 1e-12)
            rw = rw.astype(tokens.dtype)
            combine = jnp.zeros((N, E), tokens.dtype).at[jnp.arange(N)[:, None], re].set(rw)
            out = tokens
            for e in range(E):
                h = jax.nn.gelu(tokens @ w1[e] + b1[e], approximate=False)
                y = h @ w2[e] + b2[e]
                out = out + combine[:, e:e + 1] * y
            return out
        key = jax.random.key(seed)
        ks = jax.random.split(key, 4)
        scale = 1.0 / np.sqrt(D).astype(np.float32)
        return {'input_embeddings': jax.random.normal(ks[0], (B, S, D), jnp.float32), 'router_w': jax.random.normal(ks[1], (NUM_EXPERTS, D), jnp.float32) * scale, 'w1': jax.random.normal(ks[2], (NUM_EXPERTS, D, D), jnp.float32) * scale, 'b1': jnp.zeros((NUM_EXPERTS, D), jnp.float32), 'w2': jax.random.normal(ks[3], (NUM_EXPERTS, D, D), jnp.float32) * scale, 'b2': jnp.zeros((NUM_EXPERTS, D), jnp.float32)}
    _L0_ffn_all = _L0_ffn_setup()
    _L0_ffn_in = {k: v for k, v in _L0_ffn_all.items() if k in ('router_w', 'w1', 'b1', 'w2', 'b2')}
    del _L0_ffn_all
    return {'x': x, 'L0_tok_emb': _L0_tok_in['emb'], 'L0_tok_W': _L0_tok_in['W'], 'L0_tok_b': _L0_tok_in['b'], 'L0_attn_W_ih_0': _L0_attn_in['W_ih_0'], 'L0_attn_W_hh_0': _L0_attn_in['W_hh_0'], 'L0_attn_b_ih_0': _L0_attn_in['b_ih_0'], 'L0_attn_b_hh_0': _L0_attn_in['b_hh_0'], 'L0_attn_W_ih_1': _L0_attn_in['W_ih_1'], 'L0_attn_W_hh_1': _L0_attn_in['W_hh_1'], 'L0_attn_b_ih_1': _L0_attn_in['b_ih_1'], 'L0_attn_b_hh_1': _L0_attn_in['b_hh_1'], 'L0_attn_fc_w': _L0_attn_in['fc_w'], 'L0_attn_fc_b': _L0_attn_in['fc_b'], 'L0_ffn_router_w': _L0_ffn_in['router_w'], 'L0_ffn_w1': _L0_ffn_in['w1'], 'L0_ffn_b1': _L0_ffn_in['b1'], 'L0_ffn_w2': _L0_ffn_in['w2'], 'L0_ffn_b2': _L0_ffn_in['b2']}

def reference(x, L0_tok_emb, L0_tok_W, L0_tok_b, L0_attn_W_ih_0, L0_attn_W_hh_0, L0_attn_b_ih_0, L0_attn_b_hh_0, L0_attn_W_ih_1, L0_attn_W_hh_1, L0_attn_b_ih_1, L0_attn_b_hh_1, L0_attn_fc_w, L0_attn_fc_b, L0_ffn_router_w, L0_ffn_w1, L0_ffn_b1, L0_ffn_w2, L0_ffn_b2):
    import jax
    import jax.numpy as jnp

    def _L0_tok_ref(x, emb, W, b):
        import jax, jax.numpy as jnp
        import numpy as np
        INP_SIZE = 50257
        HIDDEN = 64
        KSIZE = 9
        B, T = (16, 1024)
        offsets = jnp.arange(-(KSIZE // 2), KSIZE // 2 + 1)
        idx = jnp.clip(x[..., None] + offsets, 0, INP_SIZE - 1)
        gathered = emb[idx]
        out = jnp.einsum('btkh,ohk->bto', gathered, W) + b
        return out

    def _L0_attn_ref(x, W_ih_0, W_hh_0, b_ih_0, b_hh_0, W_ih_1, W_hh_1, b_ih_1, b_hh_1, fc_w, fc_b):
        import jax, jax.numpy as jnp
        import numpy as np
        B, S, I, H, O = (64, 128, 64, 256, 64)

        def _rnn_layer(inp, W_ih, W_hh, b_ih, b_hh):
            pre = jnp.einsum('bsi,hi->bsh', inp, W_ih) + (b_ih + b_hh)
            h0 = jnp.zeros((inp.shape[0], W_hh.shape[0]), dtype=inp.dtype)

            def step(h, p_t):
                h = jnp.tanh(p_t + h @ W_hh.T)
                return (h, h)
            _, hs = jax.lax.scan(step, h0, jnp.swapaxes(pre, 0, 1))
            return jnp.swapaxes(hs, 0, 1)
        h = _rnn_layer(x, W_ih_0, W_hh_0, b_ih_0, b_hh_0)
        h = _rnn_layer(h, W_ih_1, W_hh_1, b_ih_1, b_hh_1)
        return h @ fc_w.T + fc_b

    def _L0_ffn_ref(input_embeddings, router_w, w1, b1, w2, b2):
        import jax, jax.numpy as jnp
        import numpy as np
        NUM_EXPERTS = 8
        TOP_K = 2
        B, S, D = (8, 2048, 64)

        def _moe(tokens, router_w, w1, b1, w2, b2):
            N = tokens.shape[0]
            E = router_w.shape[0]
            logits = tokens.astype(jnp.float32) @ router_w.astype(jnp.float32).T
            probs = jax.nn.softmax(logits, axis=-1)
            rw, re = jax.lax.top_k(probs, TOP_K)
            if TOP_K > 1:
                rw = rw / jnp.maximum(rw.sum(-1, keepdims=True), 1e-12)
            rw = rw.astype(tokens.dtype)
            combine = jnp.zeros((N, E), tokens.dtype).at[jnp.arange(N)[:, None], re].set(rw)
            out = tokens
            for e in range(E):
                h = jax.nn.gelu(tokens @ w1[e] + b1[e], approximate=False)
                y = h @ w2[e] + b2[e]
                out = out + combine[:, e:e + 1] * y
            return out
        b, s, d = input_embeddings.shape
        tokens = input_embeddings.reshape(b * s, d)
        return _moe(tokens, router_w, w1, b1, w2, b2).reshape(b, s, d)
    h = _L0_tok_ref(x, L0_tok_emb, L0_tok_W, L0_tok_b)
    h = h + _L0_attn_ref(_layernorm(h, axis=-1), L0_attn_W_ih_0, L0_attn_W_hh_0, L0_attn_b_ih_0, L0_attn_b_hh_0, L0_attn_W_ih_1, L0_attn_W_hh_1, L0_attn_b_ih_1, L0_attn_b_hh_1, L0_attn_fc_w, L0_attn_fc_b)
    h = h + _L0_ffn_ref(_layernorm(h, axis=-1), L0_ffn_router_w, L0_ffn_w1, L0_ffn_b1, L0_ffn_w2, L0_ffn_b2)
    return h

_drawn_inputs = setup_inputs


def setup_inputs(seed=0):
    import zlib

    import numpy as np

    out = dict(_drawn_inputs(seed))
    spreads = {'L0_ffn_b1': (0.0, 0.1), 'L0_ffn_b2': (0.0, 0.1)}
    factors = {}
    for name, (base, spread) in spreads.items():
        noise = np.random.default_rng([zlib.crc32(name.encode()), seed]).standard_normal(out[name].shape)
        drawn = base * np.exp(spread * noise) if base else spread * noise
        out[name] = jnp.asarray(drawn.astype(out[name].dtype))
    for name, factor in factors.items():
        out[name] = (out[name] * factor).astype(out[name].dtype)
    return out
```

```python
import concourse.bass as bass
from concourse import mybir
from contextlib import ExitStack

F32 = mybir.dt.float32
BF16 = mybir.dt.bfloat16
I32 = mybir.dt.int32
U32 = mybir.dt.uint32
ALU = mybir.AluOpType
ACT = mybir.ActivationFunctionType
AX = mybir.AxisListType

BATCH, TIME = 8, 256
VOCAB, D, TAPS = 50257, 64, 9
HID = 256
EXPERTS = 8
HALO = TAPS // 2
PAD = 2 * HALO
STEPS = 16
TOK = STEPS * BATCH
TILES = TIME // STEPS
SUB = 8
LAG = SUB + 1
PARTS = 3
KT = HID // 128
WIN = TAPS * D
FT = (WIN + 127) // 128
PAIRS = EXPERTS // 2
EPS = 1e-5


def hi(ap):
    return ap.bitcast(BF16)[..., 1::2]


def build(nc, ids, table, conv_w, conv_b, wih0, whh0, bih0, bhh0, wih1, whh1, bih1, bhh1,
          fc_w, fc_b, router, w1, b1, w2, b2, ident, sel, expert_no, out):
    out_v = out.rearrange("b t d -> t b d")
    with ExitStack() as ctx:
        def sb(name, shape, dt=F32):
            return ctx.enter_context(nc.sbuf_tensor(name, shape, dt))

        def bank(name):
            return ctx.enter_context(nc.psum_tensor(name, [128, 512], F32))

        def sem(name):
            return ctx.enter_context(nc.semaphore(name))

        whh_sb = [sb(f"whh{l}", [128, PARTS, KT * HID]) for l in range(2)]
        wih1_sb = sb("wih1_sb", [128, PARTS, KT * HID])
        wih0_sb = sb("wih0_sb", [D + 1, PARTS, HID])
        bias1 = sb("bias1", [1, PARTS, HID])
        b_tmp = sb("b_tmp", [D + 1, HID])
        b1_tmp = sb("b1_tmp", [1, HID])
        conv_sb = sb("conv_sb", [128, FT, D])
        fc_sb = sb("fc_sb", [128, KT, D])
        conv_bias = sb("conv_bias", [D, 1])
        fc_bias = sb("fc_bias", [D, 1])
        router_sb = sb("router_sb", [D, EXPERTS])
        w1_sb = sb("w1_sb", [D + 1, EXPERTS * D])
        w2_sb = sb("w2_sb", [128, PAIRS, D])
        b2_sb = sb("b2_sb", [EXPERTS, D])
        id_sb = sb("id_sb", [128, 128])
        sel_f = sb("sel_f", [PARTS * EXPERTS, PAIRS * 128])
        sel_sb = sb("sel_sb", [PARTS * EXPERTS, PAIRS * 128], BF16)
        eno_sb = sb("eno_sb", [128, EXPERTS])
        ones = sb("ones", [1, SUB * BATCH], BF16)
        half_neg = sb("half_neg", [128, 1])
        warm = sb("warm", [1, 1])
        ids_sb = sb("ids_sb", [TOK, TILES], I32)
        start_f = sb("start_f", [TOK, TILES])
        start_row = sb("start_row", [TOK, TILES], U32)
        row_now = sb("row_now", [TOK, 1], U32)
        window = sb("window", [TOK, WIN])
        winT = sb("winT", [128, FT, TOK])
        convT = sb("convT", [D, TOK])
        h_now = sb("h_now", [TOK, D])
        h_all = sb("h_all", [TOK, TILES * D])
        stats1, mv1, ve1, rs1 = sb("stats1", [TOK, 6]), sb("mv1", [TOK, 2]), sb("ve1", [TOK, 1]), sb("rs1", [TOK, 1])
        stats2, mv2, ve2, rs2 = sb("stats2", [TOK, 6]), sb("mv2", [TOK, 2]), sb("ve2", [TOK, 1]), sb("rs2", [TOK, 1])
        xn = sb("xn", [TOK, D + 1])
        xT = sb("xT", [D + 1, STEPS, PARTS, BATCH])
        hid = [sb(f"hid{l}", [128, STEPS, KT, PARTS, BATCH]) for l in range(2)]
        z = [sb(f"z{l}", [128, KT, BATCH]) for l in range(2)]
        fcT = sb("fcT", [D, TOK])
        h2 = sb("h2", [TOK, D])
        xn2 = sb("xn2", [TOK, D + 1])
        x2T = sb("x2T", [D + 1, TOK])
        hx = sb("hx", [TOK, D])
        top = sb("top", [TOK, 8])
        top_i = sb("top_i", [TOK, 8], U32)
        top_f = sb("top_f", [TOK, 2])
        logit = sb("logit", [TOK, EXPERTS])
        gap = sb("gap", [TOK, 2])
        rw = sb("rw", [TOK, 2])
        share = sb("share", [TOK, 2])
        c1 = sb("c1", [TOK, EXPERTS])
        c2 = sb("c2", [TOK, EXPERTS])
        comb = sb("comb", [TOK, PARTS, EXPERTS])
        combT = sb("combT", [PARTS * EXPERTS, TOK])
        act = sb("act", [128, PAIRS, TOK])
        actc = sb("actc", [128, PAIRS, TOK])
        yT = sb("yT", [D, TOK])
        o_sb = sb("o_sb", [TOK, D])

        pre = [[bank(f"pre{l}{j}") for j in range(2)] for l in range(2)]
        bank_t, bank_a, bank_f, bank_u = bank("bank_t"), bank("bank_a"), bank("bank_f"), bank("bank_u")
        pre_v = [[p[:, 0:KT * SUB * 24].rearrange("p (m s c) -> p m s c", m=KT, s=SUB) for p in pl] for pl in pre]
        winT_ps = bank_t[:, :].rearrange("p (f t) -> p f t", t=TOK)
        cb_ps = winT_ps
        win4_ps, convT_ps = bank_a[0:64, 0:128], bank_a[0:D, 128:256]
        h_ps, xT_ps = bank_a[:, 256:256 + D], bank_a[0:D + 1, 320:448]
        fcT_ps, h2_ps, x2T_ps = bank_f[0:D, 0:128], bank_f[:, 128:128 + D], bank_f[0:D + 1, 192:320]
        logit_ps, combT_ps = bank_f[:, 320:328], bank_f[0:24, 336:464]
        u_ps = bank_u[:, :].rearrange("p (e t) -> p e t", t=TOK)
        yT_ps, y_ps = bank_u[0:D, 0:128], bank_u[:, 128:128 + D]

        ld_ids, ld_rnn0, ld_rnn1, ld_conv, ld_moe, ld_misc, ld_bias = (
            sem(n) for n in ("ld_ids", "ld_rnn0", "ld_rnn1", "ld_conv", "ld_moe", "ld_misc", "ld_bias"))
        init_done, split0, split1, split_own, moe_ready, starts_ready = (
            sem(n) for n in ("init_done", "split0", "split1", "split_own", "moe_ready", "starts_ready"))
        prod_done = [sem("prod_done0"), sem("prod_done1")]
        sum_done = [sem("sum_done0"), sem("sum_done1")]
        tanh_done = [sem("tanh_done0"), sem("tanh_done1")]
        rest_done = [sem("rest_done0"), sem("rest_done1")]
        state_ready = [sem("state_ready0"), sem("state_ready1")]
        (gathered, win_t, win_sb, conv_done, conv_sb_done, h_t, h_sb, st1a, st1, var1, rs1_done, xn_done,
         xT_t, xT_sb, xT_rest, xT_done) = (sem(n) for n in (
             "gathered", "win_t", "win_sb", "conv_done", "conv_sb_done", "h_t", "h_sb", "st1a", "st1", "var1",
             "rs1_done", "xn_done", "xT_t", "xT_sb", "xT_rest", "xT_done"))
        (fc_done, fc_sb_done, h2_t, h2_done, st2a, st2, var2, rs2_done, xn2_done, x2T_t, x2T_sb, logit_done, hx_done,
         logit_sb, top_done, topi_done, gap_done, rw_done, c12, comb_hi, comb_rest, comb_done, combT_t, combT_sb,
         u_done, cb_done, index_done, act_done, actc_done, y_done, yT_sb, y_t, o_done, stored) = (sem(n) for n in (
             "fc_done", "fc_sb_done", "h2_t", "h2_done", "st2a", "st2", "var2", "rs2_done", "xn2_done", "x2T_t", "x2T_sb",
             "logit_done", "hx_done", "logit_sb", "top_done", "topi_done", "gap_done", "rw_done", "c12", "comb_hi",
             "comb_rest", "comb_done", "combT_t", "combT_sb", "u_done", "cb_done", "index_done", "act_done", "actc_done",
             "y_done", "yT_sb", "y_t", "o_done", "stored"))
        h_saved, share_done = sem("h_saved"), sem("share_done")
        block = ctx.enter_context(nc.Block())

        FULL = dict(gather=True, l0=True, l1_old=True, l1_new=True, a=True, f1=True, f2=True)

        def only(**k):
            return {**dict.fromkeys(FULL, False), **k}

        FIRST = [(-1, only(a=True, gather=True)), (0, only(l0=True, l1_new=True, a=True, gather=True)),
                 (1, {**FULL, "f2": False}), (2, FULL)]
        LAST = [(TILES - 2, {**FULL, "gather": False}), (TILES - 1, {**FULL, "a": False, "gather": False}), (TILES, only(l1_old=True, f1=True, f2=True)),
                (TILES + 1, only(f2=True))]
        LOOP = (3, TILES - 2)

        def periods(eng, body):
            for i, has in FIRST:
                body(i, has)
            with eng.Fori(*LOOP) as i:
                body(i, FULL)
            for i, has in LAST:
                body(i, has)

        def reach(eng, semaphore, value):
            if isinstance(value, int) and value <= 0:
                return
            eng.wait_ge(semaphore, value)

        def waits_apart(eng, *waits):
            eng.wait_ge(init_done, 6)
            for semaphore, value in waits:
                reach(eng, semaphore, value)

        def l1_here(has, s):
            return has["l1_old"] if s < LAG else has["l1_new"]

        @block.sync
        def _(sp):
            sp.dma_start(ids_sb[:], ids).then_inc(ld_ids, 16)
            sp.dma_start(id_sb[:], ident).then_inc(ld_conv, 16)
            sp.dma_start(wih0_sb[0:D, 0, :], wih0).then_inc(ld_bias, 16)
            sp.dma_start(wih0_sb[D:D + 1, 0, :], bih0).then_inc(ld_bias, 16)
            sp.dma_start(b_tmp[D:D + 1, :], bhh0).then_inc(ld_bias, 16)
            sp.dma_start(whh_sb[0][:, 0, :].rearrange("p (k m) -> p k m", k=KT),
                         whh0.rearrange("(k p) m -> p k m", p=128)).then_inc(ld_rnn0, 16)
            sp.dma_start(wih1_sb[:, 0, :].rearrange("p (k m) -> p k m", k=KT),
                         wih1.rearrange("(k p) m -> p k m", p=128)).then_inc(ld_rnn1, 16)
            sp.dma_start(whh_sb[1][:, 0, :].rearrange("p (k m) -> p k m", k=KT),
                         whh1.rearrange("(k p) m -> p k m", p=128)).then_inc(ld_rnn1, 16)
            sp.dma_start(bias1[0:1, 0, :], bih1).then_inc(ld_rnn1, 16)
            sp.dma_start(b1_tmp[:], bhh1).then_inc(ld_rnn1, 16)
            sp.dma_start(w1_sb[0:D, :], w1).then_inc(ld_moe, 16)
            sp.dma_start(w1_sb[D:D + 1, :], b1).then_inc(ld_moe, 16)
            sp.dma_start(w2_sb[:], w2.rearrange("(g p) d -> p g d", p=128)).then_inc(ld_moe, 16)
            sp.dma_start(b2_sb[:], b2).then_inc(ld_moe, 16)
            sp.dma_start(router_sb[:], router).then_inc(ld_moe, 16)
            sp.dma_start(sel_f[:], sel).then_inc(ld_moe, 16)
            sp.dma_start(eno_sb[:], expert_no).then_inc(ld_moe, 16)

            def store(t):
                sp.wait_ge(o_done, t + 1)
                sp.dma_start(out_v[bass.ds(t * STEPS, STEPS), :, :], o_sb[:]).then_inc(stored, 16)

            with sp.Fori(0, TILES) as t:
                store(t)
            sp.wait_ge(stored, 16 * TILES)

        @block.gpsimd
        def _(pool):
            nc.gpsimd.memset(half_neg[:], -0.5).then_inc(init_done, 1)
            nc.gpsimd.memset(xn[:, D:D + 1], 1.0).then_inc(init_done, 1)
            nc.gpsimd.memset(xn2[:, D:D + 1], 1.0).then_inc(init_done, 1)
            pool.wait_ge(init_done, 6)
            pool.wait_ge(starts_ready, 1)

            def gather(t):
                reach(pool, win_t, t)
                reach(pool, gathered, 16 * t)
                nc.gpsimd.tensor_copy(row_now[:], start_row[:, bass.ds(t, 1)])
                pool.drain()
                pool.indirect_dma_start(out=window[:, :], out_offset=None, in_=table,
                                        in_offset=bass.IndirectOffsetOnAxis(ap=row_now[:, 0:1], axis=0)
                                        ).then_inc(gathered, 16)

            gather(0)

            def body(i, has):
                if has["gather"]:
                    gather(i + 2)
                if has["f2"]:
                    t = i - 2
                    pool.wait_ge(top_done, t + 1)
                    reach(pool, rw_done, t)
                    nc.gpsimd.tensor_tensor(gap[:, 0:1], top[:, 0:1], top[:, 1:2], ALU.subtract)
                    nc.gpsimd.tensor_tensor(gap[:, 1:2], top[:, 1:2], top[:, 0:1], ALU.subtract).then_inc(gap_done, 1)
                    waits_apart(pool, (topi_done, t + 1), (rw_done, t + 1))
                    nc.gpsimd.tensor_scalar(share[:], rw[:], 0.5, 0.5, ALU.mult, ALU.add).then_inc(share_done, 1)
                    waits_apart(pool, (share_done, t + 1))
                    nc.gpsimd.tensor_scalar(c1[:], eno_sb[:], top_f[:, 0:1], share[:, 0:1], ALU.is_equal, ALU.mult)
                    nc.gpsimd.tensor_scalar(c2[:], eno_sb[:], top_f[:, 1:2], share[:, 1:2], ALU.is_equal, ALU.mult).then_inc(c12, 1)
                    pool.wait_ge(c12, t + 1)
                    reach(pool, combT_t, t)
                    nc.gpsimd.tensor_tensor(comb[:, 0, :], c1[:], c2[:], ALU.add).then_inc(comb_hi, 1)
                if has["a"]:
                    t = i + 1
                    pool.wait_ge(h_sb, t + 1)
                    nc.gpsimd.tensor_copy(h_all[:, bass.ds(t * D, D)], h_now[:]).then_inc(h_saved, 1)
                    waits_apart(pool, (st1, t + 1))
                    nc.gpsimd.tensor_scalar(ve1[:], mv1[:, 1:2], EPS, None, ALU.add).then_inc(var1, 1)
                    pool.wait_ge(var1, t + 1)
                    nc.gpsimd.tensor_tensor(rs1[:], ve1[:], half_neg[:], ALU.pow).then_inc(rs1_done, 1)
                    waits_apart(pool, (xT_t, t), (rs1_done, t + 1))
                    nc.gpsimd.tensor_scalar(xn[:, 0:D], h_now[:], mv1[:, 0:1], rs1[:], ALU.subtract, ALU.mult).then_inc(xn_done, 1)
                if has["f1"]:
                    t = i - 1
                    waits_apart(pool, (st2, t + 1))
                    nc.gpsimd.tensor_scalar(ve2[:], mv2[:, 1:2], EPS, None, ALU.add).then_inc(var2, 1)
                    pool.wait_ge(var2, t + 1)
                    nc.gpsimd.tensor_tensor(rs2[:], ve2[:], half_neg[:], ALU.pow).then_inc(rs2_done, 1)
                    waits_apart(pool, (x2T_t, t), (rs2_done, t + 1))
                    nc.gpsimd.tensor_scalar(xn2[:, 0:D], h2[:], mv2[:, 0:1], rs2[:], ALU.subtract, ALU.mult).then_inc(xn2_done, 1)
                    pool.wait_ge(xn2_done, t + 1)
                    reach(pool, o_done, t)
                    nc.gpsimd.tensor_tensor(hx[:], h2[:], xn2[:, 0:D], ALU.add).then_inc(hx_done, 1)

            periods(pool, body)

        @block.scalar
        def _(ac):
            ac.dma_start(conv_sb[:, 0:FT - 1, :], conv_w[0:(FT - 1) * 128, :].rearrange("(f p) d -> p f d", p=128)).then_inc(ld_conv, 16)
            ac.dma_start(conv_sb[0:WIN - (FT - 1) * 128, FT - 1, :], conv_w[(FT - 1) * 128:WIN, :]).then_inc(ld_conv, 16)
            ac.dma_start(fc_sb[:], fc_w.rearrange("(k p) d -> p k d", p=128)).then_inc(ld_conv, 16)
            ac.dma_start(conv_bias[:], conv_b).then_inc(ld_misc, 16)
            ac.dma_start(fc_bias[:], fc_b).then_inc(ld_misc, 16)
            ac.wait_ge(init_done, 6)
            nc.scalar.activation(warm[:], half_neg[0:1, :], ACT.Gelu)
            ac.wait_ge(ld_misc, 32)

            def tanh(l, i, s, slot):
                ac.wait_ge(sum_done[l], 16 * i + (s + 1 - LAG * l))
                nc.scalar.activation(hid[l][:, slot, :, 0, :], z[l][:], ACT.Tanh).then_inc(tanh_done[l], 1)

            def filler(i, has, s, b):
                at = (s, b)
                if has["a"]:
                    t = i + 1
                    if at in ((2, 0), (2, 1)):
                        k = 2 * b
                        ac.wait_ge(win_t, t + 1)
                        nc.scalar.copy(winT[:, k:k + 2, :], winT_ps[:, k:k + 2, :]).then_inc(win_sb, 1)
                    if at == (3, 0):
                        nc.scalar.copy(winT[0:64, 4, :], win4_ps).then_inc(win_sb, 1)
                    if at == (8, 1):
                        ac.wait_ge(conv_done, t + 1)
                        nc.scalar.activation(convT[:], convT_ps, ACT.Identity, bias=conv_bias[:]).then_inc(conv_sb_done, 1)
                    if at == (9, 1):
                        ac.wait_ge(h_t, t + 1)
                        reach(ac, xn_done, t)
                        nc.scalar.copy(h_now[:], h_ps).then_inc(h_sb, 1)
                    if at == (12, 1):
                        ac.wait_ge(xT_t, t + 1)
                        nc.scalar.copy(xT[:, :, 0, :], xT_ps.rearrange("p (s b) -> p s b", b=BATCH)).then_inc(xT_sb, 1)
                if has["f1"]:
                    t = i - 1
                    if at == (10, 0):
                        ac.wait_ge(fc_done, t + 1)
                        nc.scalar.activation(fcT[:], fcT_ps, ACT.Identity, bias=fc_bias[:]).then_inc(fc_sb_done, 1)
                    if at == (14, 1):
                        ac.wait_ge(x2T_t, t + 1)
                        nc.scalar.copy(x2T[:], x2T_ps).then_inc(x2T_sb, 1)
                if has["f2"]:
                    t = i - 2
                    if at == (1, 1):
                        ac.wait_ge(gap_done, t + 1)
                        reach(ac, c12, t)
                        nc.scalar.activation(rw[:], gap[:], ACT.Tanh, scale=0.5).then_inc(rw_done, 1)
                    if at == (5, 0):
                        ac.wait_ge(combT_t, t + 1)
                        nc.scalar.copy(combT[:], combT_ps).then_inc(combT_sb, 1)
                    if at in ((5, 1), (6, 0), (6, 1), (7, 0)):
                        g = (s * 2 + b) - 11
                        if g == 0:
                            ac.wait_ge(u_done, t + 1)
                        nc.scalar.activation(act[:, g, :], u_ps[:, g, :], ACT.Gelu).then_inc(act_done, 1)
                    if at == (13, 0):
                        ac.wait_ge(y_done, t + 1)
                        nc.scalar.copy(yT[:], yT_ps).then_inc(yT_sb, 1)

            def body(i, has):
                for s in range(STEPS):
                    if has["l0"]:
                        tanh(0, i, s, s)
                    filler(i, has, s, 0)
                    if l1_here(has, s):
                        tanh(1, i, s, (s - LAG) % STEPS)
                    filler(i, has, s, 1)

            periods(ac, body)

        @block.vector
        def _(dve):
            for l in range(2):
                nc.vector.memset(hid[l][:, STEPS - 1], 0.0).then_inc(init_done, 1)
            nc.vector.memset(ones[:], 1.0).then_inc(init_done, 1)
            dve.wait_ge(ld_ids, 16)
            nc.vector.tensor_scalar(start_f[:], ids_sb[:], float(-HALO), float(VOCAB - 1 + HALO), ALU.max, ALU.min).then_inc(split_own, 1)
            dve.wait_ge(split_own, 1)
            nc.vector.tensor_scalar(start_row[:], start_f[:], float(PAD - HALO), None, ALU.add).then_inc(starts_ready, 1)
            own = [1]

            def split(w, done):
                for p in (1, 2):
                    ins = nc.vector.tensor_tensor(w[:, p, :], w[:, p - 1, :], hi(w[:, p - 1, :]), ALU.subtract)
                    if p == 1:
                        own[0] += 1
                        ins.then_inc(split_own, 1)
                        dve.wait_ge(split_own, own[0])
                ins.then_inc(done, 1)

            dve.wait_ge(ld_bias, 48)
            nc.vector.tensor_tensor(wih0_sb[D:D + 1, 0, :], wih0_sb[D:D + 1, 0, :], b_tmp[D:D + 1, :], ALU.add).then_inc(split_own, 1)
            own[0] += 1
            dve.wait_ge(split_own, own[0])
            split(wih0_sb, split0)
            dve.wait_ge(ld_rnn0, 16)
            split(whh_sb[0], split0)

            def prepare_late():
                dve.wait_ge(ld_rnn1, 64)
                nc.vector.tensor_tensor(bias1[:, 0, :], bias1[:, 0, :], b1_tmp[:], ALU.add).then_inc(split_own, 1)
                own[0] += 1
                dve.wait_ge(split_own, own[0])
                split(bias1, split1)
                split(wih1_sb, split1)
                split(whh_sb[1], split1)
                dve.wait_ge(ld_moe, 16 * 7)
                nc.vector.tensor_copy(sel_sb[:], sel_f[:]).then_inc(moe_ready, 1)

            def count(l, i, s):
                return 16 * i + (s + 1 - LAG * l)

            def add_groups(l, i, s, slot):
                dve.wait_ge(prod_done[l], count(l, i, s))
                nc.vector.tensor_reduce(
                    z[l][:], pre_v[l][slot // SUB][:, :, slot % SUB, :].rearrange("p m (c b) -> p m b c", c=PARTS),
                    axis=AX.X, op=ALU.add).then_inc(sum_done[l], 1)

            def split_state(l, i, s, slot):
                dve.wait_ge(tanh_done[l], count(l, i, s))
                h = hid[l][:, slot]
                nc.vector.tensor_tensor(h[:, :, 1, :], h[:, :, 0, :], hi(h[:, :, 0, :]), ALU.subtract).then_inc(rest_done[l], 1)
                dve.wait_ge(rest_done[l], count(l, i, s))
                nc.vector.tensor_tensor(h[:, :, 2, :], h[:, :, 1, :], hi(h[:, :, 1, :]), ALU.subtract).then_inc(state_ready[l], 1)

            def filler(i, has, s, b):
                at = (s, b)
                if has["a"]:
                    t = i + 1
                    if at == (10, 0):
                        dve.wait_ge(h_sb, t + 1)
                        reach(dve, xn_done, t)
                        nc.vector.bn_stats(stats1[:], h_now[:]).then_inc(st1a, 1)
                    if at == (10, 1):
                        waits_apart(dve, (st1a, t + 1))
                        nc.vector.bn_aggr(mv1[:], stats1[:]).then_inc(st1, 1)
                    if at == (13, 0):
                        dve.wait_ge(xT_sb, t + 1)
                        nc.vector.tensor_tensor(xT[:, :, 1, :], xT[:, :, 0, :], hi(xT[:, :, 0, :]), ALU.subtract).then_inc(xT_rest, 1)
                    if at == (13, 1):
                        dve.wait_ge(xT_rest, t + 1)
                        nc.vector.tensor_tensor(xT[:, :, 2, :], xT[:, :, 1, :], hi(xT[:, :, 1, :]), ALU.subtract).then_inc(xT_done, 1)
                if has["f1"]:
                    t = i - 1
                    if at == (11, 0):
                        dve.wait_ge(h2_t, t + 1)
                        reach(dve, hx_done, t)
                        dve.wait_ge(h_saved, t + 1)
                        nc.vector.tensor_tensor(h2[:], h2_ps, h_all[:, bass.ds(t * D, D)], ALU.add).then_inc(h2_done, 1)
                    if at == (11, 1):
                        dve.wait_ge(h2_done, t + 1)
                        nc.vector.bn_stats(stats2[:], h2[:]).then_inc(st2a, 1)
                    if at == (12, 0):
                        waits_apart(dve, (st2a, t + 1))
                        nc.vector.bn_aggr(mv2[:], stats2[:]).then_inc(st2, 1)
                if has["f2"]:
                    t = i - 2
                    if at == (0, 0):
                        dve.wait_ge(logit_done, t + 1)
                        reach(dve, gap_done, t)
                        nc.vector.tensor_copy(logit[:], logit_ps).then_inc(logit_sb, 1)
                        waits_apart(dve, (logit_sb, t + 1))
                        nc.vector.max(top[:], logit[:]).then_inc(top_done, 1)
                    if at == (0, 1):
                        waits_apart(dve, (top_done, t + 1))
                        nc.vector.max_index(top_i[:], top[:], logit[:]).then_inc(index_done, 1)
                    if at == (1, 0):
                        dve.wait_ge(index_done, t + 1)
                        reach(dve, c12, t)
                        nc.vector.tensor_copy(top_f[:], top_i[:, 0:2]).then_inc(topi_done, 1)
                    if at == (3, 0):
                        dve.wait_ge(comb_hi, t + 1)
                        nc.vector.tensor_tensor(comb[:, 1, :], comb[:, 0, :], hi(comb[:, 0, :]), ALU.subtract).then_inc(comb_rest, 1)
                    if at == (3, 1):
                        dve.wait_ge(comb_rest, t + 1)
                        nc.vector.tensor_tensor(comb[:, 2, :], comb[:, 1, :], hi(comb[:, 1, :]), ALU.subtract).then_inc(comb_done, 1)
                    k = 2 * s + b
                    if 13 <= k < 17:
                        g = k - 13
                        dve.wait_ge(act_done, PAIRS * t + (g + 1))
                        dve.wait_ge(cb_done, t + 1)
                        nc.vector.tensor_tensor(actc[:, g, :], act[:, g, :], cb_ps[:, g, :], ALU.mult).then_inc(actc_done, 1)
                    if at == (14, 0):
                        dve.wait_ge(y_t, t + 1)
                        dve.wait_ge(hx_done, t + 1)
                        reach(dve, stored, 16 * t)
                        nc.vector.tensor_tensor(o_sb[:], y_ps, hx[:], ALU.add).then_inc(o_done, 1)

            def body(i, has):
                for s in range(STEPS):
                    slot1 = (s - LAG) % STEPS
                    if has["l0"]:
                        add_groups(0, i, s, s)
                    filler(i, has, s, 0)
                    if has["l0"]:
                        split_state(0, i, s, s)
                    if l1_here(has, s):
                        add_groups(1, i, s, slot1)
                    filler(i, has, s, 1)
                    if l1_here(has, s):
                        split_state(1, i, s, slot1)
                if isinstance(i, int) and i == -1:
                    prepare_late()

            periods(dve, body)

        @block.tensor
        def _(pe):
            mm = nc.tensor.matmul
            pe.wait_ge(init_done, 6)
            pe.wait_ge(ld_conv, 64)

            def recurrent(l, i, s, slot):
                reach(pe, state_ready[l], 16 * i + (s - LAG * l))
                prev = (slot - 1) % STEPS
                for k in range(KT):
                    moving = hi(hid[l][:, prev, k].rearrange("p c b -> p (c b)"))
                    for m in range(KT):
                        for p in range(PARTS):
                            w = hi(whh_sb[l][:, p, k * HID + m * 128:k * HID + m * 128 + 128])
                            last = mm(pre_v[l][slot // SUB][:, m, slot % SUB, :], w, moving,
                                      start=False, stop=(k == KT - 1 and p == PARTS - 1), skip_group_check=True)
                last.then_inc(prod_done[l], 1)

            def input0(j, m):
                moving = hi(xT[:, j * SUB:(j + 1) * SUB].rearrange("p s c b -> p (s c b)"))
                for p in range(PARTS):
                    mm(pre_v[0][j][:, m].rearrange("p s c -> p (s c)"), hi(wih0_sb[:, p, m * 128:m * 128 + 128]),
                       moving, start=(m == 0 and p == 0), stop=False, skip_group_check=True)

            def input1(j, m):
                dst = pre_v[1][j][:, m]
                for k in range(KT):
                    moving = hi(hid[0][:, j * SUB:(j + 1) * SUB, k].rearrange("p s c b -> p s (c b)"))
                    for p in range(PARTS):
                        mm(dst, hi(wih1_sb[:, p, k * HID + m * 128:k * HID + m * 128 + 128]), moving,
                           start=(m == 0 and k == 0 and p == 0), stop=False, skip_group_check=True)
                for p in range(PARTS):
                    mm(dst[:, :, 0:BATCH], hi(bias1[:, p, m * 128:m * 128 + 128]),
                       ones[:].rearrange("p (s b) -> p s b", b=BATCH), start=False, stop=False, skip_group_check=True)

            def fc(i, j):
                for k in range(KT):
                    last = mm(fcT_ps[:, j * SUB * BATCH:(j + 1) * SUB * BATCH], fc_sb[:, k, :],
                              hid[1][:, j * SUB:(j + 1) * SUB, k, 0, :],
                              start=(k == 0), stop=(k == KT - 1), skip_group_check=True)
                return last

            def filler(i, has, s, b):
                at = (s, b)
                if at == (0, 0) and has["l1_old"]:
                    if isinstance(i, int) and i == TILES:
                        pe.wait_ge(state_ready[0], 16 * TILES)
                    input1(1, 0)
                if at == (0, 1) and has["l1_old"]:
                    input1(1, 1)
                if s == 8 and has["l1_new"]:
                    if isinstance(i, int) and i == 0 and b == 0:
                        pe.wait_ge(split1, 3)
                    input1(0, b)
                if at == (2, 1) and has["l0"]:
                    input0(1, 0)
                if at == (3, 0) and has["l0"]:
                    input0(1, 1)
                if has["a"]:
                    t = i + 1
                    if at == (1, 0):
                        pe.wait_ge(gathered, 16 * (t + 1))
                        for f in range(3):
                            nc.tensor.transpose(winT_ps[:, f, :], window[:, f * 128:(f + 1) * 128], id_sb[:])
                    if at == (1, 1):
                        nc.tensor.transpose(winT_ps[:, 3, :], window[:, 384:512], id_sb[:])
                        nc.tensor.transpose(win4_ps, window[:, 512:576], id_sb[:]).then_inc(win_t, 1)
                    k = 2 * s + b - 11
                    if 0 <= k < FT:
                        if k == 0:
                            pe.wait_ge(win_sb, 3 * (t + 1))
                        rows = 128 if k < FT - 1 else WIN - (FT - 1) * 128
                        last = mm(convT_ps, conv_sb[0:rows, k, :], winT[0:rows, k, :], start=(k == 0), stop=(k == FT - 1))
                        if k == FT - 1:
                            last.then_inc(conv_done, 1)
                    if at == (9, 0):
                        waits_apart(pe, (conv_sb_done, t + 1))
                        nc.tensor.transpose(h_ps, convT[:], id_sb[0:D, 0:D]).then_inc(h_t, 1)
                    if at == (12, 0):
                        pe.wait_ge(xn_done, t + 1)
                        nc.tensor.transpose(xT_ps, xn[:], id_sb[:]).then_inc(xT_t, 1)
                    if at == (14, 1):
                        pe.wait_ge(xT_done, t + 1)
                        if isinstance(i, int) and i == -1:
                            pe.wait_ge(split0, 2)
                        input0(0, 0)
                    if at == (15, 0):
                        input0(0, 1)
                if has["f1"]:
                    t = i - 1
                    if at == (2, 0):
                        fc(i, 0)
                    if at == (9, 1):
                        pe.wait_ge(state_ready[1], 16 * (t + 1))
                        fc(i, 1).then_inc(fc_done, 1)
                    if at == (10, 1):
                        waits_apart(pe, (fc_sb_done, t + 1))
                        nc.tensor.transpose(h2_ps, fcT[:], id_sb[0:D, 0:D]).then_inc(h2_t, 1)
                    if at == (14, 0):
                        pe.wait_ge(xn2_done, t + 1)
                        nc.tensor.transpose(x2T_ps, xn2[:], id_sb[:]).then_inc(x2T_t, 1)
                    if at == (15, 1):
                        pe.wait_ge(x2T_sb, t + 1)
                        if isinstance(i, int) and i == 1:
                            pe.wait_ge(ld_moe, 16 * 7)
                            pe.wait_ge(moe_ready, 1)
                        mm(logit_ps, x2T[0:D, :], router_sb[:], start=True, stop=True).then_inc(logit_done, 1)
                if has["f2"]:
                    t = i - 2
                    if at in ((3, 1), (4, 0), (4, 1), (5, 0)):
                        g = 2 * s + b - 7
                        if g == 0:
                            reach(pe, o_done, t)
                        last = mm(u_ps[:, g, :], w1_sb[:, g * 128:(g + 1) * 128], x2T[:], start=True, stop=True)
                        if g == PAIRS - 1:
                            last.then_inc(u_done, 1)
                    if at == (4, 1):
                        pe.wait_ge(comb_done, t + 1)
                        nc.tensor.transpose(combT_ps, comb[:].rearrange("p c e -> p (c e)"), id_sb[:]).then_inc(combT_t, 1)
                    if at == (6, 0):
                        pe.wait_ge(combT_sb, t + 1)
                        for g in range(PAIRS):
                            last = mm(cb_ps[:, g, :], sel_sb[:, g * 128:(g + 1) * 128], hi(combT[:]), start=True, stop=True)
                        last.then_inc(cb_done, 1)
                    k = 2 * s + b - 20
                    if 0 <= k < PAIRS:
                        if k == 0:
                            pe.wait_ge(actc_done, PAIRS * (t + 1))
                        mm(yT_ps, w2_sb[:, k, :], actc[:, k, :], start=(k == 0), stop=False)
                    if k == PAIRS:
                        mm(yT_ps, b2_sb[:], combT[0:EXPERTS, :], start=False, stop=True).then_inc(y_done, 1)
                    if at == (13, 1):
                        waits_apart(pe, (yT_sb, t + 1))
                        nc.tensor.transpose(y_ps, yT[:], id_sb[0:D, 0:D]).then_inc(y_t, 1)

            def body(i, has):
                for s in range(STEPS):
                    if has["l0"]:
                        recurrent(0, i, s, s)
                    filler(i, has, s, 0)
                    if l1_here(has, s):
                        recurrent(1, i, s, (s - LAG) % STEPS)
                    filler(i, has, s, 1)

            periods(pe, body)


_NAMES = ["ids", "table", "conv_w", "conv_b", "wih0", "whh0", "bih0", "bhh0", "wih1", "whh1", "bih1", "bhh1",
          "fc_w", "fc_b", "router", "w1", "b1", "w2", "b2", "ident", "sel", "expert_no"]


def kernel(**inputs):
    import numpy as np
    import concourse.bacc as bacc
    from concourse.bass_utils import run_bass_kernel_spmd

    v = {k: np.asarray(a) for k, a in inputs.items()}
    emb = v["L0_tok_emb"]
    selector = np.zeros((PARTS, EXPERTS, PAIRS, 2, D), np.float32)
    for e in range(EXPERTS):
        selector[:, e, e // 2, e % 2, :] = 1.0
    a = {
        "ids": v["x"].T.reshape(TILES, TOK).T,
        "table": np.concatenate([np.repeat(emb[:1], PAD, 0), emb, np.repeat(emb[-1:], PAD, 0)]),
        "conv_w": v["L0_tok_W"].transpose(2, 1, 0).reshape(WIN, D),
        "conv_b": v["L0_tok_b"].reshape(D, 1),
        "wih0": v["L0_attn_W_ih_0"].T, "whh0": v["L0_attn_W_hh_0"].T,
        "bih0": v["L0_attn_b_ih_0"].reshape(1, HID), "bhh0": v["L0_attn_b_hh_0"].reshape(1, HID),
        "wih1": v["L0_attn_W_ih_1"].T, "whh1": v["L0_attn_W_hh_1"].T,
        "bih1": v["L0_attn_b_ih_1"].reshape(1, HID), "bhh1": v["L0_attn_b_hh_1"].reshape(1, HID),
        "fc_w": v["L0_attn_fc_w"].T, "fc_b": v["L0_attn_fc_b"].reshape(D, 1),
        "router": v["L0_ffn_router_w"].T,
        "w1": v["L0_ffn_w1"].transpose(1, 0, 2).reshape(D, EXPERTS * D), "b1": v["L0_ffn_b1"].reshape(1, EXPERTS * D),
        "w2": v["L0_ffn_w2"].reshape(EXPERTS * D, D), "b2": v["L0_ffn_b2"],
        "ident": np.eye(128, dtype=np.float32),
        "sel": selector.reshape(PARTS * EXPERTS, PAIRS * 128),
        "expert_no": np.tile(np.arange(EXPERTS, dtype=np.float32), (TOK, 1)),
    }
    nc = bacc.Bacc("TRN2", target_bir_lowering=False, num_devices=1)
    arrays, args = {}, []
    for name in _NAMES:
        x = np.ascontiguousarray(a[name])
        arrays[f"in_{name}"] = x
        args.append(nc.dram_tensor(f"in_{name}", x.shape, mybir.dt.from_np(x.dtype), kind="ExternalInput").ap())
    out = nc.dram_tensor("out", (BATCH, TIME, D), F32, kind="ExternalOutput").ap()
    build(nc, *args, out)
    r = run_bass_kernel_spmd(nc, [arrays], core_ids=[0])
    return r.results[0]["out"]
```

```python
import concourse.bass as bass
from concourse import mybir
from contextlib import ExitStack

F32 = mybir.dt.float32
BF16 = mybir.dt.bfloat16
I32 = mybir.dt.int32
U32 = mybir.dt.uint32
ALU = mybir.AluOpType
ACT = mybir.ActivationFunctionType
AX = mybir.AxisListType

BATCH, TIME = 8, 256
VOCAB, D, TAPS = 50257, 64, 9
HID = 256
EXPERTS = 8
HALO = TAPS // 2
PAD = 2 * HALO
STEPS = 16
TOK = STEPS * BATCH
TILES = TIME // STEPS
SUB = 8
LAG = SUB + 2
PARTS = 3
KT = HID // 128
WIN = TAPS * D
FT = (WIN + 127) // 128
PAIRS = EXPERTS // 2
EPS = 1e-5


def hi(ap):
    return ap.bitcast(BF16)[..., 1::2]


def build(nc, ids, table, conv_w, conv_b, wih0, whh0, bih0, bhh0, wih1, whh1, bih1, bhh1,
          fc_w, fc_b, router, w1, b1, w2, b2, ident, sel, expert_no, out):
    out_v = out.rearrange("b t d -> t b d")
    with ExitStack() as ctx:
        def sb(name, shape, dt=F32):
            return ctx.enter_context(nc.sbuf_tensor(name, shape, dt))

        def bank(name):
            return ctx.enter_context(nc.psum_tensor(name, [128, 512], F32))

        def sem(name):
            return ctx.enter_context(nc.semaphore(name))

        whh_sb = [sb(f"whh{l}", [128, PARTS, KT * HID]) for l in range(2)]
        wih1_sb = sb("wih1_sb", [128, KT * HID])
        wih0_sb = sb("wih0_sb", [D + 1, HID])
        bias1 = sb("bias1", [1, PARTS, HID])
        b_tmp = sb("b_tmp", [D + 1, HID])
        b1_tmp = sb("b1_tmp", [1, HID])
        conv_sb = sb("conv_sb", [128, FT, D])
        fc_sb = sb("fc_sb", [128, KT, D])
        conv_bias = sb("conv_bias", [D, 1])
        fc_bias = sb("fc_bias", [D, 1])
        router_sb = sb("router_sb", [D, EXPERTS])
        w1_sb = sb("w1_sb", [D + 1, EXPERTS * D])
        w2_sb = sb("w2_sb", [128, PAIRS, D])
        b2_sb = sb("b2_sb", [EXPERTS, D])
        id_sb = sb("id_sb", [128, 128])
        sel_f = sb("sel_f", [PARTS * EXPERTS, PAIRS * 128])
        sel_sb = sb("sel_sb", [PARTS * EXPERTS, PAIRS * 128], BF16)
        eno_sb = sb("eno_sb", [128, EXPERTS])
        ones = sb("ones", [1, SUB * BATCH], BF16)
        zeros = sb("zeros", [128, 128], BF16)
        half_neg = sb("half_neg", [128, 1])
        warm = sb("warm", [1, 1])
        ids_sb = sb("ids_sb", [TOK, TILES], I32)
        start_f = sb("start_f", [TOK, TILES])
        start_row = sb("start_row", [TOK, TILES], U32)
        row_now = sb("row_now", [TOK, 1], U32)
        window = sb("window", [TOK, WIN])
        winT = sb("winT", [128, FT, TOK])
        convT = sb("convT", [D, TOK])
        h_now = sb("h_now", [TOK, D])
        h_all = sb("h_all", [TOK, TILES * D])
        stats1, mv1, ve1, rs1 = sb("stats1", [TOK, 6]), sb("mv1", [TOK, 2]), sb("ve1", [TOK, 1]), sb("rs1", [TOK, 1])
        stats2, mv2, ve2, rs2 = sb("stats2", [TOK, 6]), sb("mv2", [TOK, 2]), sb("ve2", [TOK, 1]), sb("rs2", [TOK, 1])
        xn = sb("xn", [TOK, D + 1])
        xT = sb("xT", [D + 1, STEPS * BATCH])
        hid = [sb(f"hid{l}", [128, STEPS, KT, PARTS, BATCH]) for l in range(2)]
        z = [sb(f"z{l}", [128, KT, BATCH]) for l in range(2)]
        fcT = sb("fcT", [D, TOK])
        h2 = sb("h2", [TOK, D])
        xn2 = sb("xn2", [TOK, D + 1])
        x2T = sb("x2T", [D + 1, TOK])
        hx = sb("hx", [TOK, D])
        top = sb("top", [TOK, 8])
        top_i = sb("top_i", [TOK, 8], U32)
        top_f = sb("top_f", [TOK, 2])
        gap = sb("gap", [TOK, 2])
        rw = sb("rw", [TOK, 2])
        share = sb("share", [TOK, 2])
        c1 = sb("c1", [TOK, EXPERTS])
        c2 = sb("c2", [TOK, EXPERTS])
        comb = sb("comb", [TOK, PARTS, EXPERTS])
        combT = sb("combT", [PARTS * EXPERTS, TOK])
        act = sb("act", [128, PAIRS, TOK])
        actc = sb("actc", [128, PAIRS, TOK])
        yT = sb("yT", [D, TOK])
        o_sb = sb("o_sb", [TOK, D])

        pre = [[bank(f"pre{l}{j}") for j in range(2)] for l in range(2)]
        bank_t, bank_a, bank_f, bank_u = bank("bank_t"), bank("bank_a"), bank("bank_f"), bank("bank_u")
        pre_v = [[p[:, 0:KT * SUB * 24].rearrange("p (m s c) -> p m s c", m=KT, s=SUB) for p in pl] for pl in pre]
        winT_ps = bank_t[:, :].rearrange("p (f t) -> p f t", t=TOK)
        cb_ps = winT_ps
        win4_ps, convT_ps = bank_a[0:64, 0:128], bank_a[0:D, 128:256]
        h_ps, xT_ps = bank_a[:, 256:256 + D], bank_a[0:D + 1, 320:448]
        fcT_ps, h2_ps, x2T_ps = bank_f[0:D, 0:128], bank_f[:, 128:128 + D], bank_f[0:D + 1, 192:320]
        logit_ps, combT_ps = bank_f[:, 320:328], bank_f[0:24, 336:464]
        u_ps = bank_u[:, :].rearrange("p (e t) -> p e t", t=TOK)
        yT_ps, y_ps = bank_u[0:D, 0:128], bank_u[:, 128:128 + D]

        ld_ids, ld_rnn0, ld_rnn1, ld_conv, ld_moe, ld_misc, ld_bias = (
            sem(n) for n in ("ld_ids", "ld_rnn0", "ld_rnn1", "ld_conv", "ld_moe", "ld_misc", "ld_bias"))
        init_done, split0, split1, split_own, moe_ready, starts_ready = (
            sem(n) for n in ("init_done", "split0", "split1", "split_own", "moe_ready", "starts_ready"))
        prod_done = [sem("prod_done0"), sem("prod_done1")]
        sum_done = [sem("sum_done0"), sem("sum_done1")]
        tanh_done = [sem("tanh_done0"), sem("tanh_done1")]
        rest_done = [sem("rest_done0"), sem("rest_done1")]
        state_ready = [sem("state_ready0"), sem("state_ready1")]
        (gathered, win_t, win_sb, conv_done, conv_sb_done, h_t, h_sb, st1a, st1, var1, rs1_done, xn_done,
         xT_t, xT_sb) = (sem(n) for n in (
             "gathered", "win_t", "win_sb", "conv_done", "conv_sb_done", "h_t", "h_sb", "st1a", "st1", "var1",
             "rs1_done", "xn_done", "xT_t", "xT_sb"))
        (fc_done, fc_sb_done, h2_t, h2_done, st2a, st2, var2, rs2_done, xn2_done, x2T_t, x2T_sb, logit_done, hx_done,
         top_done, topi_done, gap_done, rw_done, c12, comb_hi, comb_rest, comb_done, combT_t, combT_sb,
         u_done, cb_done, index_done, act_done, actc_done, y_done, yT_sb, y_t, o_done, stored) = (sem(n) for n in (
             "fc_done", "fc_sb_done", "h2_t", "h2_done", "st2a", "st2", "var2", "rs2_done", "xn2_done", "x2T_t", "x2T_sb",
             "logit_done", "hx_done", "top_done", "topi_done", "gap_done", "rw_done", "c12", "comb_hi",
             "comb_rest", "comb_done", "combT_t", "combT_sb", "u_done", "cb_done", "index_done", "act_done", "actc_done",
             "y_done", "yT_sb", "y_t", "o_done", "stored"))
        h_saved, share_done = sem("h_saved"), sem("share_done")
        block = ctx.enter_context(nc.Block())

        FULL = dict(gather=True, l0=True, l1_old=True, l1_new=True, a=True, f1=True, f2=True)

        def only(**k):
            return {**dict.fromkeys(FULL, False), **k}

        FIRST = [(-1, only(a=True, gather=True)), (0, only(l0=True, l1_new=True, a=True, gather=True)),
                 (1, {**FULL, "f2": False}), (2, FULL)]
        LAST = [(TILES - 2, {**FULL, "gather": False}), (TILES - 1, {**FULL, "a": False, "gather": False}), (TILES, only(l1_old=True, f1=True, f2=True)),
                (TILES + 1, only(f2=True))]
        LOOP = (3, TILES - 2)

        def periods(eng, body):
            for i, has in FIRST:
                body(i, has)
            with eng.Fori(*LOOP) as i:
                body(i, FULL)
            for i, has in LAST:
                body(i, has)

        def reach(eng, semaphore, value):
            if isinstance(value, int) and value <= 0:
                return
            eng.wait_ge(semaphore, value)

        def waits_apart(eng, *waits):
            waits = [(semaphore, v if isinstance(v, int) else eng.to_reg(v)) for semaphore, v in waits]
            eng.wait_ge(init_done, 6)
            for semaphore, value in waits:
                reach(eng, semaphore, value)

        def l1_here(has, s):
            return has["l1_old"] if s < LAG else has["l1_new"]

        @block.sync
        def _(sp):
            sp.dma_start(ids_sb[:], ids).then_inc(ld_ids, 16)
            sp.dma_start(id_sb[:], ident).then_inc(ld_conv, 16)
            sp.dma_start(wih0_sb[0:D, :], wih0).then_inc(ld_bias, 16)
            sp.dma_start(wih0_sb[D:D + 1, :], bih0).then_inc(ld_bias, 16)
            sp.dma_start(b_tmp[D:D + 1, :], bhh0).then_inc(ld_bias, 16)
            sp.dma_start(whh_sb[0][:, 0, :].rearrange("p (k m) -> p k m", k=KT),
                         whh0.rearrange("(k p) m -> p k m", p=128)).then_inc(ld_rnn0, 16)
            sp.dma_start(wih1_sb[:].rearrange("p (k m) -> p k m", k=KT),
                         wih1.rearrange("(k p) m -> p k m", p=128)).then_inc(ld_rnn1, 16)
            sp.dma_start(whh_sb[1][:, 0, :].rearrange("p (k m) -> p k m", k=KT),
                         whh1.rearrange("(k p) m -> p k m", p=128)).then_inc(ld_rnn1, 16)
            sp.dma_start(bias1[0:1, 0, :], bih1).then_inc(ld_rnn1, 16)
            sp.dma_start(b1_tmp[:], bhh1).then_inc(ld_rnn1, 16)
            sp.dma_start(w1_sb[0:D, :], w1).then_inc(ld_moe, 16)
            sp.dma_start(w1_sb[D:D + 1, :], b1).then_inc(ld_moe, 16)
            sp.dma_start(w2_sb[:], w2.rearrange("(g p) d -> p g d", p=128)).then_inc(ld_moe, 16)
            sp.dma_start(b2_sb[:], b2).then_inc(ld_moe, 16)
            sp.dma_start(router_sb[:], router).then_inc(ld_moe, 16)
            sp.dma_start(sel_f[:], sel).then_inc(ld_moe, 16)
            sp.dma_start(eno_sb[:], expert_no).then_inc(ld_moe, 16)

            def store(t):
                sp.wait_ge(o_done, t + 1)
                sp.dma_start(out_v[bass.ds(t * STEPS, STEPS), :, :], o_sb[:]).then_inc(stored, 16)

            with sp.Fori(0, TILES) as t:
                store(t)
            sp.wait_ge(stored, 16 * TILES)

        @block.gpsimd
        def _(pool):
            nc.gpsimd.memset(half_neg[:], -0.5).then_inc(init_done, 1)
            nc.gpsimd.memset(xn[:, D:D + 1], 1.0).then_inc(init_done, 1)
            nc.gpsimd.memset(xn2[:, D:D + 1], 1.0).then_inc(init_done, 1)
            pool.wait_ge(init_done, 6)
            pool.wait_ge(starts_ready, 1)

            def gather(t):
                reach(pool, win_t, t)
                reach(pool, gathered, 16 * t)
                nc.gpsimd.tensor_copy(row_now[:], start_row[:, bass.ds(t, 1)])
                pool.drain()
                pool.indirect_dma_start(out=window[:, :], out_offset=None, in_=table,
                                        in_offset=bass.IndirectOffsetOnAxis(ap=row_now[:, 0:1], axis=0)
                                        ).then_inc(gathered, 16)

            gather(0)

            def body(i, has):
                if has["f2"]:
                    t = i - 2
                    pool.wait_ge(top_done, t + 1)
                    reach(pool, rw_done, t)
                    nc.gpsimd.tensor_tensor(gap[:, 0:1], top[:, 0:1], top[:, 1:2], ALU.subtract)
                    nc.gpsimd.tensor_tensor(gap[:, 1:2], top[:, 1:2], top[:, 0:1], ALU.subtract).then_inc(gap_done, 1)
                    waits_apart(pool, (topi_done, t + 1), (rw_done, t + 1))
                    nc.gpsimd.tensor_scalar(share[:], rw[:], 0.5, 0.5, ALU.mult, ALU.add).then_inc(share_done, 1)
                    waits_apart(pool, (share_done, t + 1))
                    nc.gpsimd.tensor_scalar(c1[:], eno_sb[:], top_f[:, 0:1], share[:, 0:1], ALU.is_equal, ALU.mult)
                    nc.gpsimd.tensor_scalar(c2[:], eno_sb[:], top_f[:, 1:2], share[:, 1:2], ALU.is_equal, ALU.mult).then_inc(c12, 1)
                    pool.wait_ge(c12, t + 1)
                    reach(pool, combT_t, t)
                    nc.gpsimd.tensor_tensor(comb[:, 0, :], c1[:], c2[:], ALU.add).then_inc(comb_hi, 1)
                if has["gather"]:
                    gather(i + 2)
                if has["a"]:
                    t = i + 1
                    pool.wait_ge(h_sb, t + 1)
                    nc.gpsimd.tensor_copy(h_all[:, bass.ds(t * D, D)], h_now[:]).then_inc(h_saved, 1)
                    waits_apart(pool, (st1, t + 1))
                    nc.gpsimd.tensor_scalar(ve1[:], mv1[:, 1:2], EPS, None, ALU.add).then_inc(var1, 1)
                    pool.wait_ge(var1, t + 1)
                    nc.gpsimd.tensor_tensor(rs1[:], ve1[:], half_neg[:], ALU.pow).then_inc(rs1_done, 1)
                    waits_apart(pool, (xT_t, t), (rs1_done, t + 1))
                    nc.gpsimd.tensor_scalar(xn[:, 0:D], h_now[:], mv1[:, 0:1], rs1[:], ALU.subtract, ALU.mult).then_inc(xn_done, 1)
                if has["f1"]:
                    t = i - 1
                    waits_apart(pool, (st2, t + 1))
                    nc.gpsimd.tensor_scalar(ve2[:], mv2[:, 1:2], EPS, None, ALU.add).then_inc(var2, 1)
                    pool.wait_ge(var2, t + 1)
                    nc.gpsimd.tensor_tensor(rs2[:], ve2[:], half_neg[:], ALU.pow).then_inc(rs2_done, 1)
                    waits_apart(pool, (x2T_t, t), (rs2_done, t + 1))
                    nc.gpsimd.tensor_scalar(xn2[:, 0:D], h2[:], mv2[:, 0:1], rs2[:], ALU.subtract, ALU.mult).then_inc(xn2_done, 1)
                    pool.wait_ge(xn2_done, t + 1)
                    reach(pool, o_done, t)
                    nc.gpsimd.tensor_tensor(hx[:], h2[:], xn2[:, 0:D], ALU.add).then_inc(hx_done, 1)

            periods(pool, body)

        @block.scalar
        def _(ac):
            ac.dma_start(conv_sb[:, 0:FT - 1, :], conv_w[0:(FT - 1) * 128, :].rearrange("(f p) d -> p f d", p=128)).then_inc(ld_conv, 16)
            ac.dma_start(conv_sb[0:WIN - (FT - 1) * 128, FT - 1, :], conv_w[(FT - 1) * 128:WIN, :]).then_inc(ld_conv, 16)
            ac.dma_start(fc_sb[:], fc_w.rearrange("(k p) d -> p k d", p=128)).then_inc(ld_conv, 16)
            ac.dma_start(conv_bias[:], conv_b).then_inc(ld_misc, 16)
            ac.dma_start(fc_bias[:], fc_b).then_inc(ld_misc, 16)
            ac.wait_ge(init_done, 6)
            nc.scalar.activation(warm[:], half_neg[0:1, :], ACT.Gelu)
            ac.wait_ge(ld_misc, 32)

            def tanh(l, i, s, slot):
                ac.wait_ge(sum_done[l], 16 * i + (s + 1 - LAG * l))
                nc.scalar.activation(hid[l][:, slot, :, 0, :], z[l][:], ACT.Tanh).then_inc(tanh_done[l], 1)

            def filler(i, has, s, b):
                at = (s, b)
                if has["a"]:
                    t = i + 1
                    if at == (3, 1):
                        ac.wait_ge(win_t, t + 1)
                        nc.scalar.copy(winT[0:64, 4, :], win4_ps).then_inc(win_sb, 1)
                    if at == (4, 0):
                        nc.scalar.copy(winT[:, 0:2, :], winT_ps[:, 0:2, :]).then_inc(win_sb, 1)
                    if at == (4, 1):
                        nc.scalar.copy(winT[:, 2:4, :], winT_ps[:, 2:4, :]).then_inc(win_sb, 1)
                    if at == (6, 0):
                        ac.wait_ge(conv_done, t + 1)
                        nc.scalar.activation(convT[:], convT_ps, ACT.Identity, bias=conv_bias[:]).then_inc(conv_sb_done, 1)
                    if at == (8, 0):
                        ac.wait_ge(h_t, t + 1)
                        reach(ac, xn_done, t)
                        nc.scalar.copy(h_now[:], h_ps).then_inc(h_sb, 1)
                    if at == (12, 1):
                        ac.wait_ge(xT_t, t + 1)
                        nc.scalar.copy(xT[:], xT_ps).then_inc(xT_sb, 1)
                if has["f1"]:
                    t = i - 1
                    if at == (11, 0):
                        ac.wait_ge(fc_done, t + 1)
                        nc.scalar.activation(fcT[:], fcT_ps, ACT.Identity, bias=fc_bias[:]).then_inc(fc_sb_done, 1)
                if has["f2"]:
                    t = i - 2
                    if at == (0, 0):
                        ac.wait_ge(x2T_t, t + 1)
                        nc.scalar.copy(x2T[:], x2T_ps).then_inc(x2T_sb, 1)
                    if at == (4, 0):
                        ac.wait_ge(gap_done, t + 1)
                        reach(ac, share_done, t)
                        nc.scalar.activation(rw[:], gap[:], ACT.Tanh, scale=0.5).then_inc(rw_done, 1)
                    if at in ((5, 0), (5, 1), (6, 1), (7, 1)):
                        g = ((5, 0), (5, 1), (6, 1), (7, 1)).index(at)
                        if g == 0:
                            ac.wait_ge(u_done, t + 1)
                        nc.scalar.activation(act[:, g, :], u_ps[:, g, :], ACT.Gelu).then_inc(act_done, 1)
                    if at == (9, 0):
                        ac.wait_ge(combT_t, t + 1)
                        nc.scalar.copy(combT[:], combT_ps).then_inc(combT_sb, 1)
                    if at == (14, 0):
                        ac.wait_ge(y_done, t + 1)
                        nc.scalar.copy(yT[:], yT_ps).then_inc(yT_sb, 1)

            def body(i, has):
                for s in range(STEPS):
                    if has["l0"]:
                        tanh(0, i, s, s)
                    filler(i, has, s, 0)
                    if l1_here(has, s):
                        tanh(1, i, s, (s - LAG) % STEPS)
                    filler(i, has, s, 1)

            periods(ac, body)

        @block.vector
        def _(dve):
            for l in range(2):
                nc.vector.memset(hid[l][:, STEPS - 1], 0.0).then_inc(init_done, 1)
            nc.vector.memset(zeros[:], 0.0)
            nc.vector.memset(ones[:], 1.0).then_inc(init_done, 1)
            dve.wait_ge(ld_ids, 16)
            nc.vector.tensor_scalar(start_f[:], ids_sb[:], float(-HALO), float(VOCAB - 1 + HALO), ALU.max, ALU.min).then_inc(split_own, 1)
            dve.wait_ge(split_own, 1)
            nc.vector.tensor_scalar(start_row[:], start_f[:], float(PAD - HALO), None, ALU.add).then_inc(starts_ready, 1)
            own = [1]

            def split(w, done):
                for p in (1, 2):
                    ins = nc.vector.tensor_tensor(w[:, p, :], w[:, p - 1, :], hi(w[:, p - 1, :]), ALU.subtract)
                    if p == 1:
                        own[0] += 1
                        ins.then_inc(split_own, 1)
                        dve.wait_ge(split_own, own[0])
                ins.then_inc(done, 1)

            dve.wait_ge(ld_bias, 48)
            nc.vector.tensor_tensor(wih0_sb[D:D + 1, :], wih0_sb[D:D + 1, :], b_tmp[D:D + 1, :], ALU.add).then_inc(split_own, 1)
            own[0] += 1
            dve.wait_ge(ld_rnn0, 16)
            split(whh_sb[0], split0)

            def prepare_late():
                dve.wait_ge(ld_rnn1, 64)
                nc.vector.tensor_tensor(bias1[:, 0, :], bias1[:, 0, :], b1_tmp[:], ALU.add).then_inc(split_own, 1)
                own[0] += 1
                dve.wait_ge(split_own, own[0])
                split(bias1, split1)
                split(whh_sb[1], split1)
                dve.wait_ge(ld_moe, 16 * 7)
                nc.vector.tensor_copy(sel_sb[:], sel_f[:]).then_inc(moe_ready, 1)

            def count(l, i, s):
                return 16 * i + (s + 1 - LAG * l)

            def add_groups(l, i, s, slot):
                dve.wait_ge(prod_done[l], count(l, i, s))
                nc.vector.tensor_reduce(
                    z[l][:], pre_v[l][slot // SUB][:, :, slot % SUB, :].rearrange("p m (c b) -> p m b c", c=PARTS),
                    axis=AX.X, op=ALU.add).then_inc(sum_done[l], 1)

            def split_state(l, i, s, slot, second):
                h = hid[l][:, slot]
                if not second:
                    dve.wait_ge(tanh_done[l], count(l, i, s))
                    nc.vector.tensor_tensor(h[:, :, 1, :], h[:, :, 0, :], hi(h[:, :, 0, :]), ALU.subtract).then_inc(rest_done[l], 1)
                else:
                    dve.wait_ge(rest_done[l], count(l, i, s))
                    nc.vector.tensor_tensor(h[:, :, 2, :], h[:, :, 1, :], hi(h[:, :, 1, :]), ALU.subtract).then_inc(state_ready[l], 1)

            def filler(i, has, s, b):
                at = (s, b)
                if has["a"]:
                    t = i + 1
                    if at == (9, 0):
                        dve.wait_ge(h_sb, t + 1)
                        reach(dve, xn_done, t)
                        nc.vector.bn_stats(stats1[:], h_now[:]).then_inc(st1a, 1)
                    if at == (9, 1):
                        waits_apart(dve, (st1a, t + 1))
                        nc.vector.bn_aggr(mv1[:], stats1[:]).then_inc(st1, 1)
                if has["f1"]:
                    t = i - 1
                    if at == (12, 1):
                        dve.wait_ge(h2_t, t + 1)
                        reach(dve, hx_done, t)
                        dve.wait_ge(h_saved, t + 1)
                        nc.vector.tensor_tensor(h2[:], h2_ps, h_all[:, bass.ds(t * D, D)], ALU.add).then_inc(h2_done, 1)
                    if at == (13, 0):
                        dve.wait_ge(h2_done, t + 1)
                        nc.vector.bn_stats(stats2[:], h2[:]).then_inc(st2a, 1)
                    if at == (13, 1):
                        waits_apart(dve, (st2a, t + 1))
                        nc.vector.bn_aggr(mv2[:], stats2[:]).then_inc(st2, 1)
                if has["f2"]:
                    t = i - 2
                    if at == (2, 1):
                        waits_apart(dve, (logit_done, t + 1))
                        nc.vector.max(top[:], logit_ps).then_inc(top_done, 1)
                    if at == (3, 0):
                        waits_apart(dve, (top_done, t + 1))
                        nc.vector.max_index(top_i[:], top[:], logit_ps).then_inc(index_done, 1)
                    if at == (3, 1):
                        dve.wait_ge(index_done, t + 1)
                        nc.vector.tensor_copy(top_f[:], top_i[:, 0:2]).then_inc(topi_done, 1)
                    if at == (6, 0):
                        dve.wait_ge(comb_hi, t + 1)
                        nc.vector.tensor_tensor(comb[:, 1, :], comb[:, 0, :], hi(comb[:, 0, :]), ALU.subtract).then_inc(comb_rest, 1)
                    if at == (6, 1):
                        dve.wait_ge(comb_rest, t + 1)
                        nc.vector.tensor_tensor(comb[:, 2, :], comb[:, 1, :], hi(comb[:, 1, :]), ALU.subtract).then_inc(comb_done, 1)
                    g = 2 * s + b - 21
                    if 0 <= g < PAIRS:
                        dve.wait_ge(act_done, PAIRS * t + (g + 1))
                        dve.wait_ge(cb_done, t + 1)
                        nc.vector.tensor_tensor(actc[:, g, :], act[:, g, :], cb_ps[:, g, :], ALU.mult).then_inc(actc_done, 1)
                    if at == (15, 0):
                        dve.wait_ge(y_t, t + 1)
                        dve.wait_ge(hx_done, t + 1)
                        reach(dve, stored, 16 * t)
                        nc.vector.tensor_tensor(o_sb[:], y_ps, hx[:], ALU.add).then_inc(o_done, 1)

            def body(i, has):
                for s in range(STEPS):
                    slot1 = (s - LAG) % STEPS
                    if l1_here(has, s - 1):
                        split_state(1, i, s - 1, (slot1 - 1) % STEPS, 0)
                    if has["l0"]:
                        add_groups(0, i, s, s)
                    if l1_here(has, s - 1):
                        split_state(1, i, s - 1, (slot1 - 1) % STEPS, 1)
                    filler(i, has, s, 0)
                    if has["l0"]:
                        split_state(0, i, s, s, 0)
                        split_state(0, i, s, s, 1)
                    if l1_here(has, s):
                        add_groups(1, i, s, slot1)
                    filler(i, has, s, 1)
                if isinstance(i, int) and i == -1:
                    prepare_late()

            periods(dve, body)

        @block.tensor
        def _(pe):
            mm = nc.tensor.matmul
            FILLED = {"l1_old": {0: 1, 2: 2}, "l1_new": {16: 1, 18: 1}, "l0": {1: 1, 3: 1},
                      "a": {5: 0, 10: 0, 11: 0, 12: 0}, "f1": {13: 0, 21: 0, 23: 1}, "f2": {7: 0, 8: 0, 9: 0, 25: 0, 26: 0}}
            KEEP = (5, 3)
            KEEP_ALONE = 12
            KEEP_APART = {(-1, 6): 16, (-1, 12): 12, (-1, 15): 28, (-1, 24): 8, (TILES, 27): 14, (TILES, 31): 6,
                          (TILES + 1, 9): 20, (TILES + 1, 14): 6, (TILES + 1, 20): 6, (TILES + 1, 26): 6}
            KEEP_START = 48

            pe.wait_ge(init_done, 6)
            for banks in pre:
                for p in banks:
                    mm(p[:, KT * SUB * 24:KT * SUB * 24 + 128], zeros[:], zeros[:], start=True, stop=True)
            for _ in range(KEEP_START):
                mm(pre[0][1][:, KT * SUB * 24:KT * SUB * 24 + 128], zeros[:], zeros[:], start=False, stop=False, skip_group_check=True)
            pe.wait_ge(ld_conv, 64)

            def recurrent(l, i, s, slot):
                reach(pe, state_ready[l], 16 * i + (s - LAG * l))
                prev = (slot - 1) % STEPS
                for k in range(KT):
                    moving = hi(hid[l][:, prev, k].rearrange("p c b -> p (c b)"))
                    for m in range(KT):
                        for p in range(PARTS):
                            w = hi(whh_sb[l][:, p, k * HID + m * 128:k * HID + m * 128 + 128])
                            last = mm(pre_v[l][slot // SUB][:, m, slot % SUB, :], w, moving,
                                      start=False, stop=(k == KT - 1 and p == PARTS - 1), skip_group_check=True)
                last.then_inc(prod_done[l], 1)

            def input0(j, m):
                mm(pre_v[0][j][:, m, :, 0:BATCH], wih0_sb[:, m * 128:m * 128 + 128],
                   xT[:, j * SUB * BATCH:(j + 1) * SUB * BATCH], start=(m == 0), stop=False, skip_group_check=True)

            def input1(j, m, k):
                dst = pre_v[1][j][:, m, :, 0:BATCH]
                mm(dst, wih1_sb[:, k * HID + m * 128:k * HID + m * 128 + 128],
                   hid[0][:, j * SUB:(j + 1) * SUB, k, 0, :], start=(m == 0 and k == 0), stop=False, skip_group_check=True)
                if k == KT - 1:
                    for p in range(PARTS):
                        mm(dst, hi(bias1[:, p, m * 128:m * 128 + 128]),
                           ones[:].rearrange("p (s b) -> p s b", b=BATCH), start=False, stop=False, skip_group_check=True)

            def fc(i, j):
                for k in range(KT):
                    last = mm(fcT_ps[:, j * SUB * BATCH:(j + 1) * SUB * BATCH], fc_sb[:, k, :],
                              hid[1][:, j * SUB:(j + 1) * SUB, k, 0, :],
                              start=(k == 0), stop=(k == KT - 1), skip_group_check=True)
                return last

            def filler(i, has, s, b):
                w = 2 * s + b
                at = (s, b)
                if w in (0, 2) and has["l1_old"]:
                    if isinstance(i, int) and i == TILES and w == 0:
                        pe.wait_ge(state_ready[0], 16 * TILES)
                    for k in range(KT):
                        input1(1, w // 2, k)
                if w in (16, 18) and has["l1_new"]:
                    if isinstance(i, int) and i == 0 and w == 16:
                        pe.wait_ge(split1, 2)
                    if w == 16:
                        pe.wait_ge(state_ready[0], 16 * i + SUB)
                    for k in range(KT):
                        input1(0, w // 2 - 8, k)
                if w in (1, 3) and has["l0"]:
                    input0(1, w // 2)
                if has["a"]:
                    t = i + 1
                    if w in (5, 6):
                        if w == 5:
                            pe.wait_ge(gathered, 16 * (t + 1))
                        for f in range(0, 2) if w == 5 else range(2, FT):
                            rows = min(128, WIN - f * 128)
                            dst = winT_ps[:, f, :] if f < FT - 1 else win4_ps
                            last = nc.tensor.transpose(dst, window[:, f * 128:f * 128 + rows], id_sb[:])
                        if f == FT - 1:
                            last.then_inc(win_t, 1)
                    if w in (10, 11, 12):
                        pe.wait_ge(win_sb, 3 * t + min(w - 8, 3))
                        for f in {10: range(0, 2), 11: range(2, 3), 12: range(3, FT)}[w]:
                            rows = min(128, WIN - f * 128)
                            last = mm(convT_ps, conv_sb[0:rows, f, :], winT[0:rows, f, :], start=(f == 0), stop=(f == FT - 1))
                        if f == FT - 1:
                            last.then_inc(conv_done, 1)
                    if at == (7, 1):
                        waits_apart(pe, (conv_sb_done, t + 1))
                        nc.tensor.transpose(h_ps, convT[:], id_sb[0:D, 0:D]).then_inc(h_t, 1)
                    if at == (12, 0):
                        pe.wait_ge(xn_done, t + 1)
                        nc.tensor.transpose(xT_ps, xn[:], id_sb[:]).then_inc(xT_t, 1)
                    if at == (14, 0):
                        pe.wait_ge(xT_sb, t + 1)
                        if isinstance(i, int) and i == -1:
                            pe.wait_ge(split_own, 2)
                            pe.wait_ge(split0, 1)
                        input0(0, 0)
                    if at == (15, 0):
                        input0(0, 1)
                if has["f1"]:
                    t = i - 1
                    if at == (6, 1):
                        reach(pe, index_done, i - 1)
                        fc(i, 0)
                    if at == (10, 1):
                        pe.wait_ge(state_ready[1], 16 * (t + 1))
                        fc(i, 1).then_inc(fc_done, 1)
                    if at == (11, 1):
                        waits_apart(pe, (fc_sb_done, t + 1))
                        nc.tensor.transpose(h2_ps, fcT[:], id_sb[0:D, 0:D]).then_inc(h2_t, 1)
                    if at == (15, 1):
                        pe.wait_ge(xn2_done, t + 1)
                        nc.tensor.transpose(x2T_ps, xn2[:], id_sb[:]).then_inc(x2T_t, 1)
                if has["f2"]:
                    t = i - 2
                    if at == (2, 0):
                        pe.wait_ge(x2T_sb, t + 1)
                        if isinstance(i, int) and i == 2:
                            pe.wait_ge(ld_moe, 16 * 7)
                            pe.wait_ge(moe_ready, 1)
                        mm(logit_ps, x2T[0:D, :], router_sb[:], start=True, stop=True).then_inc(logit_done, 1)
                    if w in (7, 8, 9):
                        if w == 7:
                            reach(pe, o_done, t)
                        for g in {7: (0,), 8: (1, 2), 9: (3,)}[w]:
                            last = mm(u_ps[:, g, :], w1_sb[:, g * 128:(g + 1) * 128], x2T[:], start=True, stop=True)
                        if w == 9:
                            last.then_inc(u_done, 1)
                    if at == (7, 0):
                        pe.wait_ge(comb_done, t + 1)
                        nc.tensor.transpose(combT_ps, comb[:].rearrange("p c e -> p (c e)"), id_sb[:]).then_inc(combT_t, 1)
                    if at == (10, 0):
                        pe.wait_ge(combT_sb, t + 1)
                        for g in range(PAIRS):
                            last = mm(cb_ps[:, g, :], sel_sb[:, g * 128:(g + 1) * 128], hi(combT[:]), start=True, stop=True)
                        last.then_inc(cb_done, 1)
                    if w in (22, 24, 25, 26):
                        g = (22, 24, 25, 26).index(w)
                        pe.wait_ge(actc_done, PAIRS * t + (g + 1))
                        mm(yT_ps, w2_sb[:, g, :], actc[:, g, :], start=(g == 0), stop=False)
                    if w == 26:
                        mm(yT_ps, b2_sb[:], combT[0:EXPERTS, :], start=False, stop=True).then_inc(y_done, 1)
                    if at == (14, 1):
                        waits_apart(pe, (yT_sb, t + 1))
                        nc.tensor.transpose(y_ps, yT[:], id_sb[0:D, 0:D]).then_inc(y_t, 1)

            def keep_clock(l, slot, n):
                dst = pre[l][1 - slot // SUB][:, KT * SUB * 24:KT * SUB * 24 + 128]
                for _ in range(n):
                    mm(dst, zeros[:], zeros[:], start=False, stop=False, skip_group_check=True)

            def keep(i, has, s, b):
                w = 2 * s + b
                layer_here = (has["l0"], l1_here(has, s))[b]
                if not layer_here:
                    if isinstance(i, int):
                        keep_clock(0, 0, KEEP_APART.get((i, w), 0))
                elif not has["l0"]:
                    keep_clock(1, (s - LAG) % STEPS, KEEP_ALONE)
                else:
                    left = [windows[w] for part, windows in FILLED.items() if has[part] and w in windows]
                    keep_clock(b, (s - LAG * b) % STEPS, min(left + [KEEP[b]]))

            def body(i, has):
                for s in range(STEPS):
                    slot1 = (s - LAG) % STEPS
                    if has["l0"]:
                        recurrent(0, i, s, s)
                    filler(i, has, s, 0)
                    keep(i, has, s, 0)
                    if l1_here(has, s):
                        recurrent(1, i, s, slot1)
                    filler(i, has, s, 1)
                    keep(i, has, s, 1)

            periods(pe, body)


_NAMES = ["ids", "table", "conv_w", "conv_b", "wih0", "whh0", "bih0", "bhh0", "wih1", "whh1", "bih1", "bhh1",
          "fc_w", "fc_b", "router", "w1", "b1", "w2", "b2", "ident", "sel", "expert_no"]


def kernel(**inputs):
    import numpy as np
    import concourse.bacc as bacc
    from concourse.bass_utils import run_bass_kernel_spmd

    v = {k: np.asarray(a) for k, a in inputs.items()}
    emb = v["L0_tok_emb"]
    selector = np.zeros((PARTS, EXPERTS, PAIRS, 2, D), np.float32)
    for e in range(EXPERTS):
        selector[:, e, e // 2, e % 2, :] = 1.0
    a = {
        "ids": v["x"].T.reshape(TILES, TOK).T,
        "table": np.concatenate([np.repeat(emb[:1], PAD, 0), emb, np.repeat(emb[-1:], PAD, 0)]),
        "conv_w": v["L0_tok_W"].transpose(2, 1, 0).reshape(WIN, D),
        "conv_b": v["L0_tok_b"].reshape(D, 1),
        "wih0": v["L0_attn_W_ih_0"].T, "whh0": v["L0_attn_W_hh_0"].T,
        "bih0": v["L0_attn_b_ih_0"].reshape(1, HID), "bhh0": v["L0_attn_b_hh_0"].reshape(1, HID),
        "wih1": v["L0_attn_W_ih_1"].T, "whh1": v["L0_attn_W_hh_1"].T,
        "bih1": v["L0_attn_b_ih_1"].reshape(1, HID), "bhh1": v["L0_attn_b_hh_1"].reshape(1, HID),
        "fc_w": v["L0_attn_fc_w"].T, "fc_b": v["L0_attn_fc_b"].reshape(D, 1),
        "router": v["L0_ffn_router_w"].T,
        "w1": v["L0_ffn_w1"].transpose(1, 0, 2).reshape(D, EXPERTS * D), "b1": v["L0_ffn_b1"].reshape(1, EXPERTS * D),
        "w2": v["L0_ffn_w2"].reshape(EXPERTS * D, D), "b2": v["L0_ffn_b2"],
        "ident": np.eye(128, dtype=np.float32),
        "sel": selector.reshape(PARTS * EXPERTS, PAIRS * 128),
        "expert_no": np.tile(np.arange(EXPERTS, dtype=np.float32), (TOK, 1)),
    }
    nc = bacc.Bacc("TRN2", target_bir_lowering=False, num_devices=1)
    arrays, args = {}, []
    for name in _NAMES:
        x = np.ascontiguousarray(a[name])
        arrays[f"in_{name}"] = x
        args.append(nc.dram_tensor(f"in_{name}", x.shape, mybir.dt.from_np(x.dtype), kind="ExternalInput").ap())
    out = nc.dram_tensor("out", (BATCH, TIME, D), F32, kind="ExternalOutput").ap()
    build(nc, *args, out)
    r = run_bass_kernel_spmd(nc, [arrays], core_ids=[0])
    return r.results[0]["out"]
```
